# Optimizing a Trainium2 kernel written in Bass

```python
import numpy as np
import jax
import jax.numpy as jnp

def _softmax(x, axis=-1):
    return jax.nn.softmax(x, axis=axis)

def _gelu(x):
    return jax.nn.gelu(x, approximate=True)

def _silu(x):
    return jax.nn.silu(x)

def _sigmoid(x):
    return jax.nn.sigmoid(x)

def _layernorm(x, axis=-1, eps=1e-05):
    m = jnp.mean(x, axis=axis, keepdims=True)
    v = jnp.var(x, axis=axis, keepdims=True)
    return (x - m) / jnp.sqrt(v + eps)

def _scatter_add(tgt, idx, src, axis=0):
    return tgt.at[idx].add(src)

def _segment_sum(src, seg, n):
    return jax.ops.segment_sum(src, seg, n)
kernel_name = 'mk_dlrm_tower_d1_rec_r8_b8f143'

def setup_inputs(seed: int=0):
    np.random.seed(seed)
    _w = jnp.asarray

    def _rec_inputs():
        import jax
        import jax.numpy as jnp
        _tk = jax.random.key(seed)
        dense_ctx = jax.random.normal(jax.random.fold_in(_tk, 190), (2048, 16), jnp.float32)
        ids = jnp.stack([jax.random.randint(jax.random.fold_in(_tk, 200 + f), (2048,), 0, v, jnp.int32) for f, v in enumerate([1000, 125000, 12500, 12500, 1000, 1250, 1000, 1000, 12500, 1000, 1000, 1000, 1250, 125000, 1000, 1000, 125000, 1250, 125000, 1250, 1250, 125000, 125000, 12500, 1000, 12500, 1000, 125000, 1250, 1000, 1000, 1000, 1250, 1000, 1250, 1250, 1250, 1000, 12500])], axis=1)
        tbl_0 = 0.05 * jax.random.normal(jax.random.fold_in(_tk, 500 + 0), (1000, 32), jnp.float32)
        tbl_1 = 0.05 * jax.random.normal(jax.random.fold_in(_tk, 500 + 1), (125000, 32), jnp.float32)
        tbl_2 = 0.05 * jax.random.normal(jax.random.fold_in(_tk, 500 + 2), (12500, 32), jnp.float32)
        tbl_3 = 0.05 * jax.random.normal(jax.random.fold_in(_tk, 500 + 3), (12500, 32), jnp.float32)
        tbl_4 = 0.05 * jax.random.normal(jax.random.fold_in(_tk, 500 + 4), (1000, 32), jnp.float32)
        tbl_5 = 0.05 * jax.random.normal(jax.random.fold_in(_tk, 500 + 5), (1250, 32), jnp.float32)
        tbl_6 = 0.05 * jax.random.normal(jax.random.fold_in(_tk, 500 + 6), (1000, 32), jnp.float32)
        tbl_7 = 0.05 * jax.random.normal(jax.random.fold_in(_tk, 500 + 7), (1000, 32), jnp.float32)
        tbl_8 = 0.05 * jax.random.normal(jax.random.fold_in(_tk, 500 + 8), (12500, 32), jnp.float32)
        tbl_9 = 0.05 * jax.random.normal(jax.random.fold_in(_tk, 500 + 9), (1000, 32), jnp.float32)
        tbl_10 = 0.05 * jax.random.normal(jax.random.fold_in(_tk, 500 + 10), (1000, 32), jnp.float32)
        tbl_11 = 0.05 * jax.random.normal(jax.random.fold_in(_tk, 500 + 11), (1000, 32), jnp.float32)
        tbl_12 = 0.05 * jax.random.normal(jax.random.fold_in(_tk, 500 + 12), (1250, 32), jnp.float32)
        tbl_13 = 0.05 * jax.random.normal(jax.random.fold_in(_tk, 500 + 13), (125000, 32), jnp.float32)
        tbl_14 = 0.05 * jax.random.normal(jax.random.fold_in(_tk, 500 + 14), (1000, 32), jnp.float32)
        tbl_15 = 0.05 * jax.random.normal(jax.random.fold_in(_tk, 500 + 15), (1000, 32), jnp.float32)
        tbl_16 = 0.05 * jax.random.normal(jax.random.fold_in(_tk, 500 + 16), (125000, 32), jnp.float32)
        tbl_17 = 0.05 * jax.random.normal(jax.random.fold_in(_tk, 500 + 17), (1250, 32), jnp.float32)
        tbl_18 = 0.05 * jax.random.normal(jax.random.fold_in(_tk, 500 + 18), (125000, 32), jnp.float32)
        tbl_19 = 0.05 * jax.random.normal(jax.random.fold_in(_tk, 500 + 19), (1250, 32), jnp.float32)
        tbl_20 = 0.05 * jax.random.normal(jax.random.fold_in(_tk, 500 + 20), (1250, 32), jnp.float32)
        tbl_21 = 0.05 * jax.random.normal(jax.random.fold_in(_tk, 500 + 21), (125000, 32), jnp.float32)
        tbl_22 = 0.05 * jax.random.normal(jax.random.fold_in(_tk, 500 + 22), (125000, 32), jnp.float32)
        tbl_23 = 0.05 * jax.random.normal(jax.random.fold_in(_tk, 500 + 23), (12500, 32), jnp.float32)
        tbl_24 = 0.05 * jax.random.normal(jax.random.fold_in(_tk, 500 + 24), (1000, 32), jnp.float32)
        tbl_25 = 0.05 * jax.random.normal(jax.random.fold_in(_tk, 500 + 25), (12500, 32), jnp.float32)
        tbl_26 = 0.05 * jax.random.normal(jax.random.fold_in(_tk, 500 + 26), (1000, 32), jnp.float32)
        tbl_27 = 0.05 * jax.random.normal(jax.random.fold_in(_tk, 500 + 27), (125000, 32), jnp.float32)
        tbl_28 = 0.05 * jax.random.normal(jax.random.fold_in(_tk, 500 + 28), (1250, 32), jnp.float32)
        tbl_29 = 0.05 * jax.random.normal(jax.random.fold_in(_tk, 500 + 29), (1000, 32), jnp.float32)
        tbl_30 = 0.05 * jax.random.normal(jax.random.fold_in(_tk, 500 + 30), (1000, 32), jnp.float32)
        tbl_31 = 0.05 * jax.random.normal(jax.random.fold_in(_tk, 500 + 31), (1000, 32), jnp.float32)
        tbl_32 = 0.05 * jax.random.normal(jax.random.fold_in(_tk, 500 + 32), (1250, 32), jnp.float32)
        tbl_33 = 0.05 * jax.random.normal(jax.random.fold_in(_tk, 500 + 33), (1000, 32), jnp.float32)
        tbl_34 = 0.05 * jax.random.normal(jax.random.fold_in(_tk, 500 + 34), (1250, 32), jnp.float32)
        tbl_35 = 0.05 * jax.random.normal(jax.random.fold_in(_tk, 500 + 35), (1250, 32), jnp.float32)
        tbl_36 = 0.05 * jax.random.normal(jax.random.fold_in(_tk, 500 + 36), (1250, 32), jnp.float32)
        tbl_37 = 0.05 * jax.random.normal(jax.random.fold_in(_tk, 500 + 37), (1000, 32), jnp.float32)
        tbl_38 = 0.05 * jax.random.normal(jax.random.fold_in(_tk, 500 + 38), (12500, 32), jnp.float32)
        _rk = jax.random.fold_in(_tk, 7)
        W_top1 = 0.0363456 * jax.random.normal(jax.random.fold_in(_tk, 801), (757, 512), jnp.float32)
        W_top2 = 0.0441942 * jax.random.normal(jax.random.fold_in(_tk, 802), (512, 256), jnp.float32)
        W_top3 = 0.0625 * jax.random.normal(jax.random.fold_in(_tk, 803), (256, 1), jnp.float32)
        b_top1 = jnp.zeros((512,), jnp.float32)
        b_top2 = jnp.zeros((256,), jnp.float32)
        return (dense_ctx, ids, tbl_0, tbl_1, tbl_2, tbl_3, tbl_4, tbl_5, tbl_6, tbl_7, tbl_8, tbl_9, tbl_10, tbl_11, tbl_12, tbl_13, tbl_14, tbl_15, tbl_16, tbl_17, tbl_18, tbl_19, tbl_20, tbl_21, tbl_22, tbl_23, tbl_24, tbl_25, tbl_26, tbl_27, tbl_28, tbl_29, tbl_30, tbl_31, tbl_32, tbl_33, tbl_34, tbl_35, tbl_36, tbl_37, tbl_38, W_top1, b_top1, W_top2, b_top2, W_top3)
    dense_ctx, ids, tbl_0, tbl_1, tbl_2, tbl_3, tbl_4, tbl_5, tbl_6, tbl_7, tbl_8, tbl_9, tbl_10, tbl_11, tbl_12, tbl_13, tbl_14, tbl_15, tbl_16, tbl_17, tbl_18, tbl_19, tbl_20, tbl_21, tbl_22, tbl_23, tbl_24, tbl_25, tbl_26, tbl_27, tbl_28, tbl_29, tbl_30, tbl_31, tbl_32, tbl_33, tbl_34, tbl_35, tbl_36, tbl_37, tbl_38, W_top1, b_top1, W_top2, b_top2, W_top3 = _rec_inputs()

    def _L0_rec_setup():
        import jax, jax.numpy as jnp
        import numpy as np
        F = 39

        def _pair_indices(f):
            row, col = ([], [])
            for i in range(f - 1):
                for j in range(i + 1, f):
                    row.append(i)
                    col.append(j)
            return (np.array(row, np.int32), np.array(col, np.int32))
        ROW, COL = _pair_indices(F)
        key = jax.random.key(seed)
        k1, k2 = jax.random.split(key)
        B, k = (1024, 32)
        P = F * (F - 1) // 2
        inputs = jax.random.normal(k1, (B, F, k), dtype=jnp.float32)
        w = jax.random.normal(k2, (k, P, k), dtype=jnp.float32)
        return {'inputs': inputs, 'w': w}
    _L0_rec_all = _L0_rec_setup()
    _L0_rec_in = {k: v for k, v in _L0_rec_all.items() if k in ('w',)}
    del _L0_rec_all
    return {'dense_ctx': dense_ctx, 'ids': ids, 'tbl_0': tbl_0, 'tbl_1': tbl_1, 'tbl_2': tbl_2, 'tbl_3': tbl_3, 'tbl_4': tbl_4, 'tbl_5': tbl_5, 'tbl_6': tbl_6, 'tbl_7': tbl_7, 'tbl_8': tbl_8, 'tbl_9': tbl_9, 'tbl_10': tbl_10, 'tbl_11': tbl_11, 'tbl_12': tbl_12, 'tbl_13': tbl_13, 'tbl_14': tbl_14, 'tbl_15': tbl_15, 'tbl_16': tbl_16, 'tbl_17': tbl_17, 'tbl_18': tbl_18, 'tbl_19': tbl_19, 'tbl_20': tbl_20, 'tbl_21': tbl_21, 'tbl_22': tbl_22, 'tbl_23': tbl_23, 'tbl_24': tbl_24, 'tbl_25': tbl_25, 'tbl_26': tbl_26, 'tbl_27': tbl_27, 'tbl_28': tbl_28, 'tbl_29': tbl_29, 'tbl_30': tbl_30, 'tbl_31': tbl_31, 'tbl_32': tbl_32, 'tbl_33': tbl_33, 'tbl_34': tbl_34, 'tbl_35': tbl_35, 'tbl_36': tbl_36, 'tbl_37': tbl_37, 'tbl_38': tbl_38, 'W_top1': W_top1, 'b_top1': b_top1, 'W_top2': W_top2, 'b_top2': b_top2, 'W_top3': W_top3, 'L0_rec_w': _L0_rec_in['w']}

def reference(dense_ctx, ids, tbl_0, tbl_1, tbl_2, tbl_3, tbl_4, tbl_5, tbl_6, tbl_7, tbl_8, tbl_9, tbl_10, tbl_11, tbl_12, tbl_13, tbl_14, tbl_15, tbl_16, tbl_17, tbl_18, tbl_19, tbl_20, tbl_21, tbl_22, tbl_23, tbl_24, tbl_25, tbl_26, tbl_27, tbl_28, tbl_29, tbl_30, tbl_31, tbl_32, tbl_33, tbl_34, tbl_35, tbl_36, tbl_37, tbl_38, W_top1, b_top1, W_top2, b_top2, W_top3, L0_rec_w):
    import jax
    import jax.numpy as jnp

    def _L0_rec_ref(inputs, w):
        import jax, jax.numpy as jnp
        import numpy as np
        F = 39

        def _pair_indices(f):
            row, col = ([], [])
            for i in range(f - 1):
                for j in range(i + 1, f):
                    row.append(i)
                    col.append(j)
            return (np.array(row, np.int32), np.array(col, np.int32))
        ROW, COL = _pair_indices(F)
        p = inputs[:, ROW, :]
        q = inputs[:, COL, :]
        return jnp.einsum('bpc,apc,bpa->bp', p, w, q)
    e = jnp.stack([tbl_0[ids[:, 0]], tbl_1[ids[:, 1]], tbl_2[ids[:, 2]], tbl_3[ids[:, 3]], tbl_4[ids[:, 4]], tbl_5[ids[:, 5]], tbl_6[ids[:, 6]], tbl_7[ids[:, 7]], tbl_8[ids[:, 8]], tbl_9[ids[:, 9]], tbl_10[ids[:, 10]], tbl_11[ids[:, 11]], tbl_12[ids[:, 12]], tbl_13[ids[:, 13]], tbl_14[ids[:, 14]], tbl_15[ids[:, 15]], tbl_16[ids[:, 16]], tbl_17[ids[:, 17]], tbl_18[ids[:, 18]], tbl_19[ids[:, 19]], tbl_20[ids[:, 20]], tbl_21[ids[:, 21]], tbl_22[ids[:, 22]], tbl_23[ids[:, 23]], tbl_24[ids[:, 24]], tbl_25[ids[:, 25]], tbl_26[ids[:, 26]], tbl_27[ids[:, 27]], tbl_28[ids[:, 28]], tbl_29[ids[:, 29]], tbl_30[ids[:, 30]], tbl_31[ids[:, 31]], tbl_32[ids[:, 32]], tbl_33[ids[:, 33]], tbl_34[ids[:, 34]], tbl_35[ids[:, 35]], tbl_36[ids[:, 36]], tbl_37[ids[:, 37]], tbl_38[ids[:, 38]]], axis=1)
    z = _L0_rec_ref(e, L0_rec_w)
    z = z.reshape(z.shape[0], -1)
    h = jnp.concatenate([z, dense_ctx], axis=1)
    h = jnp.maximum(h @ W_top1 + b_top1, 0.0)
    h = jnp.maximum(h @ W_top2 + b_top2, 0.0)
    y = h @ W_top3
    return y

_drawn_inputs = setup_inputs


def setup_inputs(seed=0):
    import zlib

    import numpy as np

    out = dict(_drawn_inputs(seed))
    spreads = {'b_top1': (0.0, 0.1), 'b_top2': (0.0, 0.1)}
    factors = {}
    for name, (base, spread) in spreads.items():
        noise = np.random.default_rng([zlib.crc32(name.encode()), seed]).standard_normal(out[name].shape)
        drawn = base * np.exp(spread * noise) if base else spread * noise
        out[name] = jnp.asarray(drawn.astype(out[name].dtype))
    for name, factor in factors.items():
        out[name] = (out[name] * factor).astype(out[name].dtype)
    return out
```

```python
import numpy as np
import concourse.bass as bass
from concourse import mybir
from contextlib import ExitStack

P = 128
F = 39
D = 32
B = 2048
NB = 512
NT = B // NB
TPG = NB // P
C = P // D
NG = -(-F // C)
DENSE = 16
H1, H2 = 512, 256
PAIRS = F * (F - 1) // 2


def fields_in(g):
    return min(C, F - C * g)


def plan():
    units, steps, first_step = [], [], []
    for g in range(NG):
        first_step.append(len(steps))
        start = len(units)
        for gi in range(g + 1):
            js = range(C * g, C * g + fields_in(g))
            for j in js if gi < g else reversed(js):
                if C * gi < j:
                    units.append((g, gi, j))
        for u in range(start, len(units), 2):
            steps.append(list(range(u, min(u + 2, len(units)))))
    first_step.append(len(steps))
    return units, steps, first_step


UNITS, STEPS, FIRST_STEP = plan()
NU, NS = len(UNITS), len(STEPS)
STEP_OF = {u: n for n, us in enumerate(STEPS) for u in us}
UPT = P // C
NZ = -(-(PAIRS + DENSE) // P)


def place_sums():
    free = [(t, v % 4, C * (v // 4)) for t in range(NZ) for v in range(UPT)
            if not (t == NZ - 1 and v % 4 == 0 and C * (v // 4) < DENSE)]
    places, behind_two, behind_three = [], None, None
    for g, gi, j in UNITS:
        n = min(C, j - C * gi)
        if n == 1 and behind_three:
            place, behind_three = behind_three, None
        elif n == 2 and behind_two and behind_two[0] == free[0][0]:
            place, behind_two = behind_two, None
        else:
            place = free.pop(0)
            tile, quad, row = place
            if n == 2:
                behind_two = (tile, quad, row + 2)
            if n == 3 or (n == 2 and fields_in(g) < C):
                behind_three = (tile, quad, row + 3)
                behind_two = behind_two if n == 3 else None
        places.append(place)
    return places


PLACES = place_sums()
WP = 8
NP = NU // WP
SELW = 2 * D - 1
R = 5
assert NU % WP == 0 and NG % R == 0 and NG % 2 == 0

SPLIT_LAG = 1

BRING = {}
for g in range(2, NG):
    BRING.setdefault(max(FIRST_STEP[g - 1], FIRST_STEP[g] - 8), g)


def at(t, per_group, n):
    return per_group * t + n


def last_step_with(gi):
    return max(STEP_OF[u] for u in range(NU) if UNITS[u][1] == gi)


def last_step_of_tile(tile):
    return max(STEP_OF[u] for u in range(NU) if PLACES[u][0] == tile)


def pieces_for(g):
    def needed(x):
        return -(-(STEPS[FIRST_STEP[x + 1] - 1][-1] + 1) // WP) if x >= 0 else 0
    return range(needed(g - 1), needed(g))


def tower(nc, tables, ids, dense, w, w1, b1, w2, b2, w3, sel_in, ident_in, y):
    F32, F32R, I32 = mybir.dt.float32, mybir.dt.float32r, mybir.dt.int32
    ALU, ACT = mybir.AluOpType, mybir.ActivationFunctionType
    IDX_A = 5 * C

    with ExitStack() as ctx:
        def sb(name, shape, dt=F32):
            return ctx.enter_context(nc.sbuf_tensor(name, shape, dt))

        def sem(name):
            return ctx.enter_context(nc.semaphore(name))

        w4 = sb("w4", [P, NU, P], F32R)
        e_rows = sb("e_rows", [P, R, TPG, P])
        eT = sb("eT", [P, NG, NB])
        parts = sb("parts", [P, 2, NB], F32R)
        e4 = sb("e4", [P, 2, C, NB], F32R)
        prod = sb("prod", [P, 4, 2, NB])
        zT = sb("zT", [P, NZ, NB])
        h1 = sb("h1", [P, H1 // P, NB])
        w1s = sb("w1s", [P, NZ, H1])
        w2s = sb("w2s", [P, H1 // P, H2])
        w3s = sb("w3s", [P, H2 // P])
        b1s = sb("b1s", [P, H1 // P])
        b2s = sb("b2s", [P, H2 // P])
        sel = sb("sel", [P, SELW])
        ident = sb("ident", [P, P])
        dense_g = sb("dense_g", [P, TPG, DENSE])
        idx_a = sb("idx_a", [P, IDX_A * TPG], I32)
        idx_b = sb("idx_b", [P, (F - IDX_A) * TPG], I32)
        stage = h1[:, :, :].rearrange("p m n -> p (m n)").rearrange("p (s n) -> p s n", s=2)
        h2 = zT[:, 0:H2 // P, :]

        y_sb = h1[0:1, 0, :]

        scratch = nc.dram_tensor("scratch", (2, C, 2, D, NB), F32, kind="Internal").ap()

        u_ps = ctx.enter_context(nc.psum_tensor("u_ps", [P, 2, 2, NB], F32))
        z_ps = ctx.enter_context(nc.psum_tensor("z_ps", [P, 2, NB], F32))
        t_ps = ctx.enter_context(nc.psum_tensor("t_ps", [P, NB], F32))
        m_ps = ctx.enter_context(nc.psum_tensor("m_ps", [P, NB], F32))
        mlp_bank = [m_ps[:, :], z_ps[:, 1, :]]

        s_const = sem("s_const")
        s_mlpw = sem("s_mlpw")
        s_idxa = sem("s_idxa")
        s_idxb = sem("s_idxb")
        s_dense = sem("s_dense")
        s_rows = [sem(f"s_rows{r}") for r in range(R)]
        s_tp = sem("s_tp")
        s_eh = sem("s_eh")
        s_et = sem("s_et")
        s_el = sem("s_el")
        s_scr = sem("s_scr")
        s_e4 = [sem("s_e40"), sem("s_e41")]
        s_stage = [sem("s_stage0"), sem("s_stage1")]
        s_wh = sem("s_wh")
        s_wl = sem("s_wl")
        s_held = sem("s_held")
        s_pad = sem("s_pad")
        s_u = sem("s_u")
        s_mul = sem("s_mul")
        s_red = sem("s_red")
        s_z = sem("s_z")
        s_zc = sem("s_zc")
        s_m = sem("s_m")
        s_mc = sem("s_mc")
        s_y = sem("s_y")

        NI = H1 // P + H2 // P + 1
        ROWS = 16 * TPG
        E4 = 16 * 2
        E4_GROUP = E4 * NG // 2

        def rows_count(g):
            return ROWS * sum(fields_in(x) for x in range(g % R, g + 1, R))

        def rows_group(g):
            return rows_count(NG - R + g % R)

        def e4_count(g):
            return E4 * (g // 2 + 1)

        def hold(eng):
            eng.sem_inc(s_held, 1)

        block = ctx.enter_context(nc.Block())

        @block.gpsimd
        def _(pool):
            def group(t, first):
                for g in range(NG):
                    if g == 0:
                        pool.wait_ge(s_idxa, at(t, 16, 16))
                        hold(pool)
                    if C * g == IDX_A:
                        pool.wait_ge(s_idxb, at(t, 16, 16))
                        hold(pool)
                    if not first or g >= R:
                        pool.wait_ge(s_tp, at(t, NG, g - R + 1))
                        hold(pool)
                    for q in range(fields_in(g)):
                        f = C * g + q
                        idx, col = (idx_a, f * TPG) if f < IDX_A else (idx_b, (f - IDX_A) * TPG)
                        for n in range(TPG):
                            pool.indirect_dma_start(
                                e_rows[:, g % R, n, D * q:D * q + D], None, tables[f],
                                bass.IndirectOffsetOnAxis(ap=idx[:, col + n:col + n + 1], axis=0),
                            ).then_inc(s_rows[g % R], 16)

            group(0, True)
            with pool.Fori(1, NT) as t:
                group(t, False)

        @block.sync
        def _(sp):
            def load_piece(k):
                if k >= NP:
                    return
                if k >= 2:
                    sp.wait_ge(s_wl, k - 1)
                for r in range(4):
                    sp.dma_start(stage[D * r:D * r + D, k % 2, :],
                                 w[:, k * WP * P:(k + 1) * WP * P]).then_inc(s_stage[k % 2], 16)

            def stack_chunk(t, g, first):
                nj = fields_in(g)
                here = scratch[g % 2, 0:nj]
                if not first or g >= 2:
                    sp.wait_ge(s_e4[g % 2], at(t, E4_GROUP, e4_count(g) - E4))
                    hold(sp)
                sp.wait_ge(s_eh, at(t, NG, g + 1))
                hold(sp)
                sp.dma_start(here[:, 0], parts[0:D * nj, 0, :].bitcast(F32)).then_inc(s_scr, 16)
                sp.wait_ge(s_el, at(t, NG, g + 1))
                hold(sp)
                sp.dma_start(here[:, 1], parts[0:D * nj, 1, :].bitcast(F32)).then_inc(s_scr, 16)
                if not first or g >= 2:
                    sp.wait_ge(s_u, at(t, NS, FIRST_STEP[g - 1] if g >= 2 else FIRST_STEP[NG - 1 + g] - NS))
                    hold(sp)
                sp.wait_ge(s_scr, at(t, 32 * NG, 32 * (g + 1)))
                hold(sp)
                for r in range(2):
                    sp.dma_start(e4[2 * D * r:2 * D * (r + 1), g % 2, 0:nj, :].bitcast(F32),
                                 here.rearrange("j h a n -> (h a) j n")).then_inc(s_e4[g % 2], 16)

            def group(t, first):
                if not first:
                    sp.wait_ge(s_z, at(t, 1, 0))
                    hold(sp)
                    sp.wait_ge(s_tp, at(t, NG, 0))
                    hold(sp)
                dense_rows = dense[0:1] if first else dense[bass.ds(t, 1)]
                idx_rows = ids[0:1] if first else ids[bass.ds(t, 1)]
                next_rows = ids[1:2] if first else ids[bass.ds(t + 1, 1)]
                sp.dma_start(idx_b[:, :], idx_rows[:, :, IDX_A * TPG:].rearrange("t p n -> p (t n)")).then_inc(s_idxb, 16)
                sp.dma_start(dense_g[:, :, :], dense_rows.rearrange("t p n d -> p (t n) d")).then_inc(s_dense, 16)
                for g in range(NG):
                    if first:
                        for k in pieces_for(g):
                            load_piece(k + 2)
                    stack_chunk(t, g, first)
                    if C * (g + 1) == IDX_A:
                        sp.dma_start(idx_a[:, :], next_rows[:, :, 0:IDX_A * TPG].rearrange("t p n -> p (t n)")).then_inc(s_idxa, 16)

            sp.dma_start(idx_a[:, :], ids[0, :, 0:IDX_A * TPG]).then_inc(s_idxa, 16)
            sp.dma_start(ident[:, :], ident_in).then_inc(s_const, 16)
            load_piece(0)
            sp.dma_start(sel[:, :], sel_in).then_inc(s_const, 16)
            load_piece(1)
            group(0, True)
            with sp.Fori(1, NT) as t:
                group(t, False)
            sp.wait_ge(s_idxa, 16 * (NT + 1))

        @block.tensor
        def _(pe):
            def transpose_chunk(t, g, first):
                pe.wait_ge(s_rows[g % R], at(t, rows_group(g), rows_count(g)))
                if not first or g >= 1:
                    pe.wait_ge(s_et, at(t, NG, g))
                n = D * fields_in(g)
                for b in range(TPG):
                    last = nc.tensor.transpose(t_ps[0:n, b * P:b * P + P], e_rows[:, g % R, b, 0:n], ident[:, :])
                last.then_inc(s_tp, 1)

            def interact(t, n, first):
                g = UNITS[STEPS[n][0]][0]
                if n in FIRST_STEP:
                    pe.wait_ge(s_e4[g % 2], at(t, E4_GROUP, e4_count(g)))
                    if first:
                        pe.wait_ge(s_wl, max(pieces_for(g), default=0) + 1)
                if n >= 2:
                    pe.wait_ge(s_mul, at(t, NS, n - 1))
                for i, u in enumerate(STEPS[n]):
                    last = nc.tensor.matmul(u_ps[:, n % 2, i, :], w4[:, u, :], e4[:, g % 2, UNITS[u][2] - C * g, :],
                                            start=True, stop=True)
                last.then_inc(s_u, 1)

            def reduce(t, batch, first):
                pe.wait_ge(s_mul, at(t, NS, batch[-1] + 1))
                for n in batch:
                    for i, u in enumerate(STEPS[n]):
                        tile, quad, row = PLACES[u]
                        opens = (tile, quad) not in [x[:2] for x in PLACES[:u]]
                        closes = (tile, quad) not in [x[:2] for x in PLACES[u + 1:]] and (tile, quad) != (NZ - 1, 0)
                        if tile >= 2 and tile not in [x[0] for x in PLACES[:u]]:
                            pe.wait_ge(s_zc, at(t, NZ, tile - 1))
                        last = nc.tensor.matmul(z_ps[D * quad:D * quad + D, tile % 2, :],
                                                sel[:, D - 1 - row:2 * D - 1 - row], prod[:, n % 4, i, :],
                                                start=opens, stop=closes, skip_group_check=True)
                    last.then_inc(s_red, 1)

            def add_dense(t):
                pe.wait_ge(s_dense, at(t, 16, 16))
                for b in range(TPG):
                    last = nc.tensor.matmul(z_ps[0:DENSE, (NZ - 1) % 2, b * P:b * P + P], dense_g[:, b, :],
                                            ident[:, :], start=False, stop=b == TPG - 1, skip_group_check=True)
                last.then_inc(s_z, 1)

            def layer_1(t):
                pe.wait_ge(s_mlpw, 16 * 5)
                pe.wait_ge(s_zc, at(t, NZ, NZ))
                for m in range(H1 // P):
                    if m >= 2:
                        pe.wait_ge(s_mc, at(t, NI, m - 1))
                    for k in range(NZ):
                        last = nc.tensor.matmul(mlp_bank[m % 2], w1s[:, k, m * P:m * P + P], zT[:, k, :],
                                                start=k == 0, stop=k == NZ - 1)
                    last.then_inc(s_m, 1)

            def layers_2_and_3(t):
                pe.wait_ge(s_mc, at(t, NI, H1 // P))
                for m in range(H2 // P):
                    for k in range(H1 // P):
                        last = nc.tensor.matmul(mlp_bank[m % 2], w2s[:, k, m * P:m * P + P], h1[:, k, :],
                                                start=k == 0, stop=k == H1 // P - 1)
                    last.then_inc(s_m, 1)
                pe.wait_ge(s_mc, at(t, NI, NI - 1))
                for k in range(H2 // P):
                    last = nc.tensor.matmul(m_ps[0:1, :], w3s[:, k:k + 1], h2[:, k, :],
                                            start=k == 0, stop=k == H2 // P - 1)
                last.then_inc(s_m, 1)

            def group(t, first):
                transpose_chunk(t, 0, first)
                if not first:
                    layer_1(t - 1)
                transpose_chunk(t, 1, first)
                if not first:
                    layers_2_and_3(t - 1)
                for n in range(0, NS + 2, 2):
                    for x in range(n, min(n + 2, NS)):
                        if x in BRING:
                            transpose_chunk(t, BRING[x], first)
                        interact(t, x, first)
                    if n >= 2:
                        reduce(t, range(n - 2, min(n, NS)), first)
                add_dense(t)

            pe.wait_ge(s_const, 32)
            group(0, True)
            with pe.Fori(1, NT) as t:
                group(t, False)
            layer_1(NT - 1)
            layers_2_and_3(NT - 1)

        @block.scalar
        def _(act):
            def take_chunk(t, g, first):
                n = D * fields_in(g)
                if not first or g >= 1:
                    act.wait_ge(s_scr, at(t, 32 * NG, 32 * g))
                act.wait_ge(s_tp, at(t, NG, g + 1))
                nc.scalar.copy(parts[0:n, 0, :], t_ps[0:n, :]).then_inc(s_eh, 1)
                if not first:
                    act.wait_ge(s_mul, at(t, NS, last_step_with(g) + 1 - NS))
                nc.scalar.copy(eT[0:n, g, :], t_ps[0:n, :]).then_inc(s_et, 1)

            def weights_high(k):
                act.wait_ge(s_stage[k % 2], 64 * (k // 2 + 1))
                nc.scalar.copy(w4[:, k * WP:(k + 1) * WP, :].rearrange("p u n -> p (u n)"),
                               stage[:, k % 2, :]).then_inc(s_wh, 1)

            def take_z(t, tile, first):
                if tile < NZ - 1:
                    act.wait_ge(s_red, at(t, NS, last_step_of_tile(tile) + 1))
                else:
                    act.wait_ge(s_z, at(t, 1, 1))
                if not first and tile == 0:
                    act.wait_ge(s_m, at(t, NI, 0))
                nc.scalar.copy(zT[:, tile, :], z_ps[:, tile % 2, :]).then_inc(s_zc, 1)

            def take_h1(t):
                for m in range(H1 // P):
                    act.wait_ge(s_m, at(t, NI, m + 1))
                    nc.scalar.activation(h1[:, m, :], mlp_bank[m % 2], ACT.Relu,
                                         bias=b1s[:, m:m + 1]).then_inc(s_mc, 1)

            def take_h2_and_y(t, dst):
                for m in range(H2 // P):
                    act.wait_ge(s_m, at(t, NI, H1 // P + m + 1))
                    nc.scalar.activation(h2[:, m, :], mlp_bank[m % 2], ACT.Relu,
                                         bias=b2s[:, m:m + 1]).then_inc(s_mc, 1)
                act.wait_ge(s_m, at(t, NI, NI))
                nc.scalar.copy(y_sb, m_ps[0:1, :]).then_inc(s_mc, 1)
                act.wait_ge(s_mc, at(t, NI, NI))
                act.sem_inc(s_held, 1)
                act.dma_start(dst, y_sb).then_inc(s_y, 16)

            def group(t, first):
                if first:
                    for k in pieces_for(0):
                        weights_high(k)
                take_chunk(t, 0, first)
                if first:
                    for k in pieces_for(1):
                        weights_high(k)
                else:
                    take_h1(t - 1)
                take_chunk(t, 1, first)
                if not first:
                    take_h2_and_y(t - 1, y[bass.ds(t - 1, 1), :])
                for n in range(0, NS + 2, 2):
                    for x in (n, n + 1):
                        if x in BRING:
                            if first:
                                for k in pieces_for(BRING[x]):
                                    weights_high(k)
                            take_chunk(t, BRING[x], first)
                    for tile in range(NZ - 1):
                        if last_step_of_tile(tile) in (n - 2, n - 1):
                            take_z(t, tile, first)
                take_z(t, NZ - 1, first)
                if not first:
                    act.wait_ge(s_y, at(t, 16, 0))

            for dst, src in ((w1s[:, :, :], w1), (w2s[:, :, :], w2), (w3s[:, :], w3), (b1s[:, :], b1), (b2s[:, :], b2)):
                act.dma_start(dst, src).then_inc(s_mlpw, 16)
            group(0, True)
            act.wait_ge(s_mlpw, 16 * 5)
            with act.Fori(1, NT) as t:
                group(t, False)
            take_h1(NT - 1)
            take_h2_and_y(NT - 1, y[NT - 1:NT, :])
            act.wait_ge(s_y, 16 * NT)

        @block.vector
        def _(dve):
            def split_chunk(t, g, first):
                n = D * fields_in(g)
                dve.wait_ge(s_et, at(t, NG, g + 1))
                nc.vector.tensor_tensor(parts[0:n, 1, :], eT[0:n, g, :], parts[0:n, 0, :].bitcast(F32),
                                        ALU.subtract).then_inc(s_el, 1)

            def weights_low(k):
                dve.wait_ge(s_wh, k + 1)
                piece = w4[P // 2:P, k * WP:(k + 1) * WP, :].rearrange("p u n -> p (u n)")
                nc.vector.tensor_tensor(piece, stage[P // 2:P, k % 2, :], piece.bitcast(F32),
                                        ALU.subtract).then_inc(s_wl, 1)

            def multiply(t, n, first):
                dve.wait_ge(s_u, at(t, NS, n + 1))
                if n >= 4:
                    dve.wait_ge(s_red, at(t, NS, n - 3))
                elif n == 0 and not first:
                    dve.wait_ge(s_red, at(t, NS, 0))
                k = len(STEPS[n])
                gi = [UNITS[u][1] for u in STEPS[n]]
                e = eT[:, gi[0]:gi[-1] + 1, :]
                if k == 2 and gi[0] == gi[1]:
                    e = e.broadcast_to([P, 2, NB])
                nc.vector.tensor_tensor(prod[:, n % 4, 0:k, :], u_ps[:, n % 2, 0:k, :], e,
                                        ALU.mult).then_inc(s_mul, 1)

            def group(t, first):
                for g in (0, 1):
                    if first:
                        for k in pieces_for(g):
                            weights_low(k)
                    split_chunk(t, g, first)
                for n in range(NS):
                    if n - SPLIT_LAG in BRING:
                        g = BRING[n - SPLIT_LAG]
                        if first:
                            for k in pieces_for(g):
                                weights_low(k)
                        split_chunk(t, g, first)
                    multiply(t, n, first)

            nc.vector.memset(eT[D * fields_in(NG - 1):P, NG - 1, :], 0.0).then_inc(s_pad, 1)
            dve.wait_ge(s_pad, 1)
            group(0, True)
            with dve.Fori(1, NT) as t:
                group(t, False)


def kernel(**inputs):
    import numpy as _np
    import concourse.bacc as _bacc
    from concourse import mybir as _mybir
    from concourse.bass_utils import run_bass_kernel_spmd as _run

    nc = _bacc.Bacc("TRN2", target_bir_lowering=False, num_devices=1)
    arrays = {}

    def give(name, a):
        a = _np.ascontiguousarray(a)
        arrays[f"in_{name}_dram"] = a
        return nc.dram_tensor(f"in_{name}_dram", a.shape, _mybir.dt.from_np(a.dtype), kind="ExternalInput").ap()

    tables = [give(f"tbl_{f}", inputs[f"tbl_{f}"]) for f in range(F)]

    ids = _np.asarray(inputs["ids"])
    by_group = ids.reshape(NT, TPG, P, F).transpose(0, 2, 3, 1).reshape(NT, P, F * TPG)
    ids_in = give("ids", _np.concatenate([by_group, _np.zeros_like(by_group[:1])]))
    dense = _np.asarray(inputs["dense_ctx"]).reshape(NT, TPG, P, DENSE).transpose(0, 2, 1, 3)
    dense_in = give("dense", dense)

    w = _np.asarray(inputs["L0_rec_w"])
    w1 = _np.asarray(inputs["W_top1"])
    w_units = _np.zeros((D, NU, C, D), w.dtype)
    w1_rows = _np.zeros((NZ * P, H1), w1.dtype)
    for u, (g, gi, j) in enumerate(UNITS):
        tile, quad, row = PLACES[u]
        for q in range(min(C, j - C * gi)):
            i = C * gi + q
            pair = i * F - i * (i + 1) // 2 + j - i - 1
            w_units[:, u, q, :] = w[:, pair, :]
            w1_rows[tile * P + D * quad + row + q] = w1[pair]
    w1_rows[(NZ - 1) * P:(NZ - 1) * P + DENSE] = w1[PAIRS:]
    w_in = give("w", w_units.reshape(D, NU * P))
    w1_in = give("w1", w1_rows.reshape(NZ, P, H1).transpose(1, 0, 2))
    w2_in = give("w2", _np.asarray(inputs["W_top2"]).reshape(H1 // P, P, H2).transpose(1, 0, 2))
    w3_in = give("w3", _np.asarray(inputs["W_top3"]).reshape(H2 // P, P).T)
    b1_in = give("b1", _np.asarray(inputs["b_top1"]).reshape(H1 // P, P).T)
    b2_in = give("b2", _np.asarray(inputs["b_top2"]).reshape(H2 // P, P).T)

    sel = _np.zeros((P, SELW), _np.float32)
    for p in range(P):
        sel[p, D - 1 + p // D] = 1.0
    sel_in = give("sel", sel)
    ident_in = give("ident", _np.eye(P, dtype=_np.float32))

    y = nc.dram_tensor("out_y_dram", (NT, NB), _mybir.dt.float32, kind="ExternalOutput").ap()
    tower(nc, tables, ids_in, dense_in, w_in, w1_in, b1_in, w2_in, b2_in, w3_in, sel_in, ident_in, y)
    r = _run(nc, [arrays], core_ids=[0])
    return r.results[0]["out_y_dram"].reshape(B, 1)
```

```python
import numpy as np
import concourse.bass as bass
from concourse import mybir
from contextlib import ExitStack

P = 128
F = 39
D = 32
B = 2048
NB = 512
NT = B // NB
TPG = NB // P
C = P // D
NG = -(-F // C)
DENSE = 16
H1, H2 = 512, 256
PAIRS = F * (F - 1) // 2


def fields_in(g):
    return min(C, F - C * g)


def plan():
    units, steps, first_step = [], [], []
    for g in range(NG):
        first_step.append(len(steps))
        start = len(units)
        for gi in range(g + 1):
            js = range(C * g, C * g + fields_in(g))
            for j in js if gi < g else reversed(js):
                if C * gi < j:
                    units.append((g, gi, j))
        for u in range(start, len(units), 2):
            steps.append(list(range(u, min(u + 2, len(units)))))
    first_step.append(len(steps))
    return units, steps, first_step


UNITS, STEPS, FIRST_STEP = plan()
NU, NS = len(UNITS), len(STEPS)
STEP_OF = {u: n for n, us in enumerate(STEPS) for u in us}
UPT = P // C
NZ = -(-(PAIRS + DENSE) // P)


def place_sums():
    free = [(t, v % 4, C * (v // 4)) for t in range(NZ) for v in range(UPT)
            if not (t == NZ - 1 and v % 4 == 0 and C * (v // 4) < DENSE)]
    places, behind_two, behind_three = [], None, None
    for g, gi, j in UNITS:
        n = min(C, j - C * gi)
        if n == 1 and behind_three:
            place, behind_three = behind_three, None
        elif n == 2 and behind_two and behind_two[0] == free[0][0]:
            place, behind_two = behind_two, None
        else:
            place = free.pop(0)
            tile, quad, row = place
            if n == 2:
                behind_two = (tile, quad, row + 2)
            if n == 3 or (n == 2 and fields_in(g) < C):
                behind_three = (tile, quad, row + 3)
                behind_two = behind_two if n == 3 else None
        places.append(place)
    return places


PLACES = place_sums()
WP = 8
NP = NU // WP
SELW = 2 * D - 1
R = 5
assert NU % WP == 0 and NG % R == 0 and NG % 2 == 0

PER_TWO = 4
LATER = 4
LEAD = 10
SPLIT_LAG = 1



BRING = {}
for g in range(2, NG):
    BRING.setdefault(max(FIRST_STEP[g - 1], FIRST_STEP[g] - LEAD), []).append(g)


def last_step_with(gi):
    return max(STEP_OF[u] for u in range(NU) if UNITS[u][1] == gi)


NEXT = {last_step_with(g) + 3: g for g in (0, 1)}
NEXT_LAG = 2


START = {g: x for x, gs in BRING.items() for g in gs} | {NG: NS}
START[2] = 0


def at(t, per_group, n):
    return per_group * t + n


MLP = ([(1, m, k) for m in range(H1 // P) for k in range(NZ)]
       + [(2, m, k) for m in range(H2 // P) for k in range(H1 // P)]
       + [(3, 0, k) for k in range(H2 // P)])
LAYER_INPUTS = {1: NZ, 2: H1 // P, 3: H2 // P}
ITEM = {(1, m): m for m in range(H1 // P)} | {(2, m): H1 // P + m for m in range(H2 // P)} | {(3, 0): H1 // P + H2 // P}
NI = len(ITEM)


def mlp_pieces(batch):
    first_layer = NZ * H1 // P

    def until(x):
        swift = x * PER_TWO // 2
        if swift < first_layer:
            return swift
        return min(len(MLP), first_layer + max(0, x * LATER // 4 - (2 * first_layer // PER_TWO) * LATER // 4))
    return MLP[until(batch):until(batch + 1)]


Z_FREE = next(b for b in range(NS) if (1, H1 // P - 1, NZ - 1) in mlp_pieces(b))


def last_step_of_tile(tile):
    return max(STEP_OF[u] for u in range(NU) if PLACES[u][0] == tile)


def pieces_at(n):
    return [k for k in range(2, NP) if 3 * (k - 2) == n]


for n in range(NS):
    assert 2 + sum(len(pieces_at(x)) for x in range(n + 1)) > STEPS[n][-1] // WP


def tower(nc, tables, ids, dense, w, w1, b1, w2, b2, w3, sel_in, ident_in, y):
    F32, F32R, I32 = mybir.dt.float32, mybir.dt.float32r, mybir.dt.int32
    ALU, ACT = mybir.AluOpType, mybir.ActivationFunctionType
    IDX_A = 5 * C

    with ExitStack() as ctx:
        def sb(name, shape, dt=F32):
            return ctx.enter_context(nc.sbuf_tensor(name, shape, dt))

        def sem(name):
            return ctx.enter_context(nc.semaphore(name))

        w4 = sb("w4", [P, NU, P], F32R)
        e_rows = sb("e_rows", [P, R, TPG, P])
        eT = sb("eT", [P, NG, NB])
        parts = sb("parts", [P, 2, 2, NB], F32R)
        e4 = sb("e4", [P, 2, C, NB], F32R)
        prod = sb("prod", [P, 4, 2, NB])
        zT = sb("zT", [P, NZ, NB])
        h1 = sb("h1", [P, H1 // P, NB])
        w1s = sb("w1s", [P, NZ, H1])
        w2s = sb("w2s", [P, H1 // P, H2])
        w3s = sb("w3s", [P, H2 // P])
        b1s = sb("b1s", [P, H1 // P])
        b2s = sb("b2s", [P, H2 // P])
        sel = sb("sel", [P, SELW])
        ident = sb("ident", [P, P])
        dense_g = sb("dense_g", [P, TPG, DENSE])
        idx_a = sb("idx_a", [P, IDX_A * TPG], I32)
        idx_b = sb("idx_b", [P, (F - IDX_A) * TPG], I32)
        stage = h1[:, :, :].rearrange("p m n -> p (m n)").rearrange("p (s n) -> p s n", s=2)
        h2 = zT[:, NZ - H2 // P:NZ, :]

        y_sb = h1[0:1, 0, :]

        scratch = nc.dram_tensor("scratch", (2, C, 2, D, NB), F32, kind="Internal").ap()

        u_ps = ctx.enter_context(nc.psum_tensor("u_ps", [P, 2, 2, NB], F32))
        z_ps = ctx.enter_context(nc.psum_tensor("z_ps", [P, 2, NB], F32))
        t_ps = ctx.enter_context(nc.psum_tensor("t_ps", [P, NB], F32))
        m_ps = ctx.enter_context(nc.psum_tensor("m_ps", [P, NB], F32))

        s_const = sem("s_const")
        s_mlpw = sem("s_mlpw")
        s_idxa = sem("s_idxa")
        s_idxb = sem("s_idxb")
        s_dense = sem("s_dense")
        s_rows = [sem(f"s_rows{r}") for r in range(R)]
        s_tp = sem("s_tp")
        s_eh = sem("s_eh")
        s_et = sem("s_et")
        s_el = sem("s_el")
        s_scr = sem("s_scr")
        s_e4 = [sem("s_e40"), sem("s_e41")]
        s_stage = [sem("s_stage0"), sem("s_stage1")]
        s_wh = sem("s_wh")
        s_wl = sem("s_wl")
        s_held = sem("s_held")
        s_pad = sem("s_pad")
        s_u = sem("s_u")
        s_mul = sem("s_mul")
        s_red = sem("s_red")
        s_z = sem("s_z")
        s_zc = sem("s_zc")
        s_m = sem("s_m")
        s_mc = sem("s_mc")
        s_y = sem("s_y")

        ROWS = 16 * TPG
        E4 = 16 * 2
        E4_GROUP = E4 * NG // 2

        def rows_count(g):
            return ROWS * sum(fields_in(x) for x in range(g % R, g + 1, R))

        def rows_group(g):
            return rows_count(NG - R + g % R)

        def e4_count(g):
            return E4 * (g // 2 + 1)

        def hold(eng):
            eng.sem_inc(s_held, 1)

        block = ctx.enter_context(nc.Block())

        @block.gpsimd
        def _(pool):
            def group(t, first):
                for g in range(NG):
                    if g == 0:
                        pool.wait_ge(s_idxa, at(t, 16, 16))
                        hold(pool)
                    if C * g == IDX_A:
                        pool.wait_ge(s_idxb, at(t, 16, 16))
                        hold(pool)
                    if not first or g >= R:
                        pool.wait_ge(s_tp, at(t, NG, g - R + 1))
                        hold(pool)
                    for q in range(fields_in(g)):
                        f = C * g + q
                        idx, col = (idx_a, f * TPG) if f < IDX_A else (idx_b, (f - IDX_A) * TPG)
                        for n in range(TPG):
                            pool.indirect_dma_start(
                                e_rows[:, g % R, n, D * q:D * q + D], None, tables[f],
                                bass.IndirectOffsetOnAxis(ap=idx[:, col + n:col + n + 1], axis=0),
                            ).then_inc(s_rows[g % R], 16)

            group(0, True)
            with pool.Fori(1, NT) as t:
                group(t, False)

        @block.sync
        def _(sp):
            def load_piece(k):
                if k >= NP:
                    return
                if k >= 2:
                    sp.wait_ge(s_wl, k - 1)
                for r in range(4):
                    sp.dma_start(stage[D * r:D * r + D, k % 2, :],
                                 w[:, k * WP * P:(k + 1) * WP * P]).then_inc(s_stage[k % 2], 16)

            def stack_chunk(t, g, first):
                nj = fields_in(g)
                here = scratch[g % 2, 0:nj]
                if not first or g >= 2:
                    sp.wait_ge(s_e4[g % 2], at(t, E4_GROUP, e4_count(g) - E4))
                    hold(sp)
                sp.wait_ge(s_eh, at(t, NG, g + 1))
                hold(sp)
                sp.dma_start(here[:, 0], parts[0:D * nj, g % 2, 0, :].bitcast(F32)).then_inc(s_scr, 16)
                sp.wait_ge(s_el, at(t, NG, g + 1))
                hold(sp)
                sp.dma_start(here[:, 1], parts[0:D * nj, g % 2, 1, :].bitcast(F32)).then_inc(s_scr, 16)
                if not first or g >= 2:
                    sp.wait_ge(s_u, at(t, NS, FIRST_STEP[g - 1] if g >= 2 else FIRST_STEP[NG - 1 + g] - NS))
                    hold(sp)
                sp.wait_ge(s_scr, at(t, 32 * NG, 32 * (g + 1)))
                hold(sp)
                for r in range(2):
                    sp.dma_start(e4[2 * D * r:2 * D * (r + 1), g % 2, 0:nj, :].bitcast(F32),
                                 here.rearrange("j h a n -> (h a) j n")).then_inc(s_e4[g % 2], 16)

            def group(t, first, last):
                if not first:
                    sp.wait_ge(s_z, at(t, 1, 0))
                    hold(sp)
                    sp.wait_ge(s_tp, at(t, NG, 0))
                    hold(sp)
                dense_rows = dense[t:t + 1] if isinstance(t, int) else dense[bass.ds(t, 1)]
                idx_rows = ids[t:t + 1] if isinstance(t, int) else ids[bass.ds(t, 1)]
                if not last:
                    next_rows = ids[t + 1:t + 2] if isinstance(t, int) else ids[bass.ds(t + 1, 1)]
                sp.dma_start(idx_b[:, :], idx_rows[:, :, IDX_A * TPG:].rearrange("t p n -> p (t n)")).then_inc(s_idxb, 16)
                sp.dma_start(dense_g[:, :, :], dense_rows.rearrange("t p n d -> p (t n) d")).then_inc(s_dense, 16)
                for g in range(0 if first else 2, NG):
                    stack_chunk(t, g, first)
                    if first and g < 2:
                        load_piece(g + 2)
                    elif first:
                        for n in range(START[g], START[g + 1]):
                            for k in pieces_at(n):
                                load_piece(k + 2)
                    if C * (g + 1) == IDX_A and not last:
                        sp.dma_start(idx_a[:, :], next_rows[:, :, 0:IDX_A * TPG].rearrange("t p n -> p (t n)")).then_inc(s_idxa, 16)
                if not last:
                    for g in (0, 1):
                        stack_chunk(t + 1, g, False)

            sp.dma_start(idx_a[:, :], ids[0, :, 0:IDX_A * TPG]).then_inc(s_idxa, 16)
            sp.dma_start(ident[:, :], ident_in).then_inc(s_const, 16)
            load_piece(0)
            sp.dma_start(sel[:, :], sel_in).then_inc(s_const, 16)
            load_piece(1)
            group(0, True, False)
            with sp.Fori(1, NT - 1) as t:
                group(t, False, False)
            group(NT - 1, False, True)

        @block.tensor
        def _(pe):
            def transpose_chunk(t, g, first):
                pe.wait_ge(s_rows[g % R], at(t, rows_group(g), rows_count(g)))
                if not first or g >= 1:
                    pe.wait_ge(s_et, at(t, NG, g))
                n = D * fields_in(g)
                for b in range(TPG):
                    last = nc.tensor.transpose(t_ps[0:n, b * P:b * P + P], e_rows[:, g % R, b, 0:n], ident[:, :])
                last.then_inc(s_tp, 1)

            def interact(t, n, first):
                g = UNITS[STEPS[n][0]][0]
                if n in FIRST_STEP:
                    pe.wait_ge(s_e4[g % 2], at(t, E4_GROUP, e4_count(g)))
                if first and (n == 0 or STEPS[n][-1] // WP > STEPS[n - 1][-1] // WP):
                    pe.wait_ge(s_wl, STEPS[n][-1] // WP + 1)
                if n >= 2:
                    pe.wait_ge(s_mul, at(t, NS, n - 1))
                for i, u in enumerate(STEPS[n]):
                    last = nc.tensor.matmul(u_ps[:, n % 2, i, :], w4[:, u, :], e4[:, g % 2, UNITS[u][2] - C * g, :],
                                            start=True, stop=True)
                last.then_inc(s_u, 1)

            def reduce(t, batch, first):
                pe.wait_ge(s_mul, at(t, NS, batch[-1] + 1))
                for n in batch:
                    for i, u in enumerate(STEPS[n]):
                        tile, quad, row = PLACES[u]
                        opens = (tile, quad) not in [x[:2] for x in PLACES[:u]]
                        closes = (tile, quad) not in [x[:2] for x in PLACES[u + 1:]] and (tile, quad) != (NZ - 1, 0)
                        if tile >= 2 and tile not in [x[0] for x in PLACES[:u]]:
                            pe.wait_ge(s_zc, at(t, NZ, tile - 1))
                        last = nc.tensor.matmul(z_ps[D * quad:D * quad + D, tile % 2, :],
                                                sel[:, D - 1 - row:2 * D - 1 - row], prod[:, n % 4, i, :],
                                                start=opens, stop=closes, skip_group_check=True)
                    last.then_inc(s_red, 1)

            def add_dense(t):
                pe.wait_ge(s_dense, at(t, 16, 16))
                for b in range(TPG):
                    last = nc.tensor.matmul(z_ps[0:DENSE, (NZ - 1) % 2, b * P:b * P + P], dense_g[:, b, :],
                                            ident[:, :], start=False, stop=b == TPG - 1, skip_group_check=True)
                last.then_inc(s_z, 1)

            def mlp_piece(t, layer, m, k):
                if (layer, m, k) == (1, 0, 0):
                    pe.wait_ge(s_mlpw, 16 * 5)
                    pe.wait_ge(s_zc, at(t, NZ, NZ))
                elif k == 0:
                    pe.wait_ge(s_mc, at(t, NI, ITEM[layer, m]))
                stop = k == LAYER_INPUTS[layer] - 1
                if layer == 1:
                    last = nc.tensor.matmul(m_ps[:, :], w1s[:, k, m * P:m * P + P], zT[:, k, :], start=k == 0, stop=stop)
                elif layer == 2:
                    last = nc.tensor.matmul(m_ps[:, :], w2s[:, k, m * P:m * P + P], h1[:, k, :], start=k == 0, stop=stop)
                else:
                    last = nc.tensor.matmul(m_ps[0:1, :], w3s[:, k:k + 1], h2[:, k, :], start=k == 0, stop=stop)
                if stop:
                    last.then_inc(s_m, 1)

            def group(t, first, last):
                if first:
                    transpose_chunk(t, 0, first)
                    transpose_chunk(t, 1, first)
                for n in range(0, NS + 2, 2):
                    for x in range(n, min(n + 2, NS)):
                        for g in BRING.get(x, ()):
                            transpose_chunk(t, g, first)
                        if x in NEXT and not last:
                            transpose_chunk(t + 1, NEXT[x], False)
                        interact(t, x, first)
                        if not first:
                            pieces = mlp_pieces(n // 2)
                            half = len(pieces) // 2
                            for piece in pieces[:half] if x == n else pieces[half:]:
                                mlp_piece(t - 1, *piece)
                    if n >= 2:
                        reduce(t, range(n - 2, min(n, NS)), first)
                add_dense(t)

            pe.wait_ge(s_const, 32)
            group(0, True, False)
            with pe.Fori(1, NT - 1) as t:
                group(t, False, False)
            group(NT - 1, False, True)
            for piece in MLP:
                mlp_piece(NT - 1, *piece)

        @block.scalar
        def _(act):
            def take_chunk(t, g, first):
                n = D * fields_in(g)
                if not first or g >= 2:
                    act.wait_ge(s_scr, at(t, 32 * NG, 32 * (g - 1)))
                act.wait_ge(s_tp, at(t, NG, g + 1))
                nc.scalar.copy(parts[0:n, g % 2, 0, :], t_ps[0:n, :]).then_inc(s_eh, 1)
                if not first:
                    act.wait_ge(s_mul, at(t, NS, last_step_with(g) + 1 - NS))
                nc.scalar.copy(eT[0:n, g, :], t_ps[0:n, :]).then_inc(s_et, 1)

            def weights_high(k):
                act.wait_ge(s_stage[k % 2], 64 * (k // 2 + 1))
                nc.scalar.copy(w4[:, k * WP:(k + 1) * WP, :].rearrange("p u n -> p (u n)"),
                               stage[:, k % 2, :]).then_inc(s_wh, 1)

            def take_z(t, tile, first):
                if tile < NZ - 1:
                    act.wait_ge(s_red, at(t, NS, last_step_of_tile(tile) + 1))
                else:
                    act.wait_ge(s_z, at(t, 1, 1))
                if not first and tile == 0:
                    act.wait_ge(s_m, at(t - 1, NI, H1 // P))
                nc.scalar.copy(zT[:, tile, :], z_ps[:, tile % 2, :]).then_inc(s_zc, 1)

            def take_mlp(t, layer, m, dst):
                act.wait_ge(s_m, at(t, NI, ITEM[layer, m] + 1))
                if layer == 1:
                    nc.scalar.activation(h1[:, m, :], m_ps[:, :], ACT.Relu, bias=b1s[:, m:m + 1]).then_inc(s_mc, 1)
                elif layer == 2:
                    nc.scalar.activation(h2[:, m, :], m_ps[:, :], ACT.Relu, bias=b2s[:, m:m + 1]).then_inc(s_mc, 1)
                else:
                    nc.scalar.copy(y_sb, m_ps[0:1, :]).then_inc(s_mc, 1)
                    act.wait_ge(s_mc, at(t, NI, NI))
                    act.sem_inc(s_held, 1)
                    act.dma_start(dst, y_sb).then_inc(s_y, 16)

            def group(t, first, last):
                if first:
                    for g in (0, 1):
                        take_chunk(t, g, first)
                        weights_high(g)
                for n in range(0, NS + 2, 2):
                    for x in (n, n + 1):
                        for g in BRING.get(x, ()):
                            take_chunk(t, g, first)
                        if first:
                            for k in pieces_at(x):
                                weights_high(k)
                        if x in NEXT and not last:
                            take_chunk(t + 1, NEXT[x], False)
                    if not first:
                        for layer, m, k in mlp_pieces(n // 2):
                            if k == LAYER_INPUTS[layer] - 1:
                                take_mlp(t - 1, layer, m, y[t - 1:t, :] if last else y[bass.ds(t - 1, 1), :])
                    for tile in range(NZ - 1):
                        if max(last_step_of_tile(tile) // 2 + 1, Z_FREE) == n // 2:
                            take_z(t, tile, first)
                take_z(t, NZ - 1, first)
                if not first:
                    act.wait_ge(s_y, at(t, 16, 0))

            for dst, src in ((w1s[:, :, :], w1), (w2s[:, :, :], w2), (w3s[:, :], w3), (b1s[:, :], b1), (b2s[:, :], b2)):
                act.dma_start(dst, src).then_inc(s_mlpw, 16)
            group(0, True, False)
            act.wait_ge(s_mlpw, 16 * 5)
            with act.Fori(1, NT - 1) as t:
                group(t, False, False)
            group(NT - 1, False, True)
            for layer, m in ITEM:
                take_mlp(NT - 1, layer, m, y[NT - 1:NT, :])
            act.wait_ge(s_y, 16 * NT)

        @block.vector
        def _(dve):
            def split_chunk(t, g, first):
                n = D * fields_in(g)
                dve.wait_ge(s_et, at(t, NG, g + 1))
                nc.vector.tensor_tensor(parts[0:n, g % 2, 1, :], eT[0:n, g, :], parts[0:n, g % 2, 0, :].bitcast(F32),
                                        ALU.subtract).then_inc(s_el, 1)

            def weights_low(k):
                dve.wait_ge(s_wh, k + 1)
                piece = w4[P // 2:P, k * WP:(k + 1) * WP, :].rearrange("p u n -> p (u n)")
                nc.vector.tensor_tensor(piece, stage[P // 2:P, k % 2, :], piece.bitcast(F32),
                                        ALU.subtract).then_inc(s_wl, 1)

            def multiply(t, n, first):
                dve.wait_ge(s_u, at(t, NS, n + 1))
                if n >= 4:
                    dve.wait_ge(s_red, at(t, NS, n - 3))
                elif n == 0 and not first:
                    dve.wait_ge(s_red, at(t, NS, 0))
                k = len(STEPS[n])
                gi = [UNITS[u][1] for u in STEPS[n]]
                e = eT[:, gi[0]:gi[-1] + 1, :]
                if k == 2 and gi[0] == gi[1]:
                    e = e.broadcast_to([P, 2, NB])
                nc.vector.tensor_tensor(prod[:, n % 4, 0:k, :], u_ps[:, n % 2, 0:k, :], e,
                                        ALU.mult).then_inc(s_mul, 1)

            def group(t, first, last):
                if first:
                    for g in (0, 1):
                        split_chunk(t, g, first)
                        weights_low(g)
                for n in range(NS):
                    for g in BRING.get(n - SPLIT_LAG, ()):
                        split_chunk(t, g, first)
                    if first:
                        for k in pieces_at(n):
                            weights_low(k)
                    if n - NEXT_LAG in NEXT and not last:
                        split_chunk(t + 1, NEXT[n - NEXT_LAG], False)
                    multiply(t, n, first)

            nc.vector.memset(eT[D * fields_in(NG - 1):P, NG - 1, :], 0.0).then_inc(s_pad, 1)
            dve.wait_ge(s_pad, 1)
            group(0, True, False)
            with dve.Fori(1, NT - 1) as t:
                group(t, False, False)
            group(NT - 1, False, True)


def kernel(**inputs):
    import numpy as _np
    import concourse.bacc as _bacc
    from concourse import mybir as _mybir
    from concourse.bass_utils import run_bass_kernel_spmd as _run

    nc = _bacc.Bacc("TRN2", target_bir_lowering=False, num_devices=1)
    arrays = {}

    def give(name, a):
        a = _np.ascontiguousarray(a)
        arrays[f"in_{name}_dram"] = a
        return nc.dram_tensor(f"in_{name}_dram", a.shape, _mybir.dt.from_np(a.dtype), kind="ExternalInput").ap()

    tables = [give(f"tbl_{f}", inputs[f"tbl_{f}"]) for f in range(F)]

    ids = _np.asarray(inputs["ids"])
    ids_in = give("ids", ids.reshape(NT, TPG, P, F).transpose(0, 2, 3, 1).reshape(NT, P, F * TPG))
    dense = _np.asarray(inputs["dense_ctx"]).reshape(NT, TPG, P, DENSE).transpose(0, 2, 1, 3)
    dense_in = give("dense", dense)

    w = _np.asarray(inputs["L0_rec_w"])
    w1 = _np.asarray(inputs["W_top1"])
    w_units = _np.zeros((D, NU, C, D), w.dtype)
    w1_rows = _np.zeros((NZ * P, H1), w1.dtype)
    for u, (g, gi, j) in enumerate(UNITS):
        tile, quad, row = PLACES[u]
        for q in range(min(C, j - C * gi)):
            i = C * gi + q
            pair = i * F - i * (i + 1) // 2 + j - i - 1
            w_units[:, u, q, :] = w[:, pair, :]
            w1_rows[tile * P + D * quad + row + q] = w1[pair]
    w1_rows[(NZ - 1) * P:(NZ - 1) * P + DENSE] = w1[PAIRS:]
    w_in = give("w", w_units.reshape(D, NU * P))
    w1_in = give("w1", w1_rows.reshape(NZ, P, H1).transpose(1, 0, 2))
    w2_in = give("w2", _np.asarray(inputs["W_top2"]).reshape(H1 // P, P, H2).transpose(1, 0, 2))
    w3_in = give("w3", _np.asarray(inputs["W_top3"]).reshape(H2 // P, P).T)
    b1_in = give("b1", _np.asarray(inputs["b_top1"]).reshape(H1 // P, P).T)
    b2_in = give("b2", _np.asarray(inputs["b_top2"]).reshape(H2 // P, P).T)

    sel = _np.zeros((P, SELW), _np.float32)
    for p in range(P):
        sel[p, D - 1 + p // D] = 1.0
    sel_in = give("sel", sel)
    ident_in = give("ident", _np.eye(P, dtype=_np.float32))

    y = nc.dram_tensor("out_y_dram", (NT, NB), _mybir.dt.float32, kind="ExternalOutput").ap()
    tower(nc, tables, ids_in, dense_in, w_in, w1_in, b1_in, w2_in, b2_in, w3_in, sel_in, ident_in, y)
    r = _run(nc, [arrays], core_ids=[0])
    return r.results[0]["out_y_dram"].reshape(B, 1)
```

```python
import numpy as np
import concourse.bass as bass
from concourse import mybir
from contextlib import ExitStack

P = 128
F = 39
D = 32
B = 2048
NB = 256
NT = B // NB
TPG = NB // P
C = P // D
NG = -(-F // C)
DENSE = 16
H1, H2 = 512, 256
PAIRS = F * (F - 1) // 2

HG, HOT = 7, 3
HP, HK = 125, 8
OS = 3


def fields_in(g):
    return min(C, F - C * g)


def gathered(g, first):
    return fields_in(g) - HOT if g == HG and not first else fields_in(g)


def plan():
    units, steps, first_step = [], [], []
    for g in range(NG):
        first_step.append(len(steps))
        for gi in range(g + 1):
            js = range(C * g, C * g + fields_in(g))
            step = [(g, gi, j) for j in (js if gi < g else reversed(js)) if C * gi < j]
            steps.append(list(range(len(units), len(units) + len(step))))
            units += step
    first_step.append(len(steps))
    return units, steps, first_step


UNITS, STEPS, FIRST_STEP = plan()
NU, NS = len(UNITS), len(STEPS)
STEP_OF = {u: n for n, us in enumerate(STEPS) for u in us}
UPT = P // C
NZ = -(-(PAIRS + DENSE) // P)


def place_sums():
    free = [(t, v % 4, C * (v // 4)) for t in range(NZ) for v in range(UPT)
            if not (t == NZ - 1 and v % 4 == 0 and C * (v // 4) < DENSE)]
    places, behind_two, behind_three = [], None, None
    for g, gi, j in UNITS:
        n = min(C, j - C * gi)
        if n == 1 and behind_three:
            place, behind_three = behind_three, None
        elif n == 2 and behind_two and behind_two[0] == free[0][0]:
            place, behind_two = behind_two, None
        else:
            place = free.pop(0)
            tile, quad, row = place
            if n == 2:
                behind_two = (tile, quad, row + 2)
            if n == 3 or (n == 2 and fields_in(g) < C):
                behind_three = (tile, quad, row + 3)
                behind_two = behind_two if n == 3 else None
        places.append(place)
    return places


PLACES = place_sums()
WP = 8
NP = NU // WP
WS = 4
SELW = 2 * D - 1
R = 5
ES = 5
assert NU % WP == 0 and NG % R == 0 and NG % ES == 0 and NT % 2 == 0

BS = 2
PER_EIGHT = 12
PER_TWO = 4
LATER = 4
EARLY_PER_BATCH = 2
LEAD = 9
LEAD_FIRST = 10
LEAD_LAST = 7
SPLIT_LAG = 1
AHEAD = 4
XE = 2
NEXT_AT, NEXT_BY = 40, 3
AFTER = 3
NEXT_LAG = 1
PS = 2
HOT_LEAD = 2
BEFORE = 7


def last_step_with(gi):
    return FIRST_STEP[NG - 1] + gi


NEXT = {NEXT_AT + NEXT_BY * g if g < XE else last_step_with(g) + AFTER: g for g in range(AHEAD)}


def bring(first, last):
    steps = {}
    for g in range(2 if first else AHEAD, NG):
        if first:
            step = max(FIRST_STEP[g - 1], FIRST_STEP[g] - LEAD_FIRST)
        else:
            step = max(0, FIRST_STEP[g] - (LEAD_LAST if last else LEAD))
        steps.setdefault(step, []).append(g)
    return steps


def look_up(last):
    step = {g: x for x, gs in bring(False, last).items() for g in gs}
    return [min(step[HG - 1] + 1 + k, step[HG] - 1) for k in range(HK)]


START = {g: x for x, gs in bring(True, False).items() for g in gs} | {NG: NS}
START[2] = 0


def at(t, per_group, n):
    return per_group * t + n


MLP = ([(1, m, k) for m in range(H1 // P) for k in range(NZ)]
       + [(2, m, k) for m in range(H2 // P) for k in range(H1 // P)]
       + [(3, 0, k) for k in range(H2 // P)])
LAYER_INPUTS = {1: NZ, 2: H1 // P, 3: H2 // P}
ITEM = {(1, m): m for m in range(H1 // P)} | {(2, m): H1 // P + m for m in range(H2 // P)} | {(3, 0): H1 // P + H2 // P}
NI = len(ITEM)


def mlp_pieces(batch, last):
    first_layer = NZ * H1 // P

    def until(x):
        if not last:
            return min(len(MLP), x * PER_EIGHT // 8)
        swift = x * PER_TWO // 2
        if swift < first_layer:
            return swift
        return min(len(MLP), first_layer + max(0, x * LATER // 4 - (2 * first_layer // PER_TWO) * LATER // 4))
    return MLP[until(batch):until(batch + 1)]


def last_step_of_tile(tile):
    return max(STEP_OF[u] for u in range(NU) if PLACES[u][0] == tile)


def early_pieces():
    bank_free = [max(b for b in range(NS) if mlp_pieces(b, True)) + 2, max(bring(False, True)) // BS + 2,
                 last_step_of_tile(NZ - 2) // BS + 2, (NS - 1) // BS]
    by_batch = {}
    for ready, m, k in sorted((max(bank_free[m], last_step_of_tile(k) // BS + 2), m, k)
                              for m in range(H1 // P) for k in range(NZ - 1)):
        while len(by_batch.get(ready, ())) == EARLY_PER_BATCH and ready < (NS - 1) // BS:
            ready += 1
        by_batch.setdefault(ready, []).append((m, k))
    return by_batch


def pieces_at(n):
    return [k for k in range(2, NP) if 2 * (k - 2) == n]


EARLY = early_pieces()

for n in range(NS):
    assert 2 + sum(len(pieces_at(x)) for x in range(n + 1)) > STEPS[n][-1] // WP


def tower(nc, tables, ids, hot_ids, hot_rows, dense, w, w1, b1, w2, b2, w3, sel_in, ident_in, y):
    F32, F32R, I32 = mybir.dt.float32, mybir.dt.float32r, mybir.dt.int32
    ALU, ACT = mybir.AluOpType, mybir.ActivationFunctionType
    IDX_A = 5 * C

    with ExitStack() as ctx:
        def sb(name, shape, dt=F32):
            return ctx.enter_context(nc.sbuf_tensor(name, shape, dt))

        def sem(name):
            return ctx.enter_context(nc.semaphore(name))

        w4 = sb("w4", [P, NU, P], F32R)
        e_rows = sb("e_rows", [P, R, TPG, P])
        eT = sb("eT", [P, NG + XE, NB])
        parts = sb("parts", [P, PS, 2, NB], F32R)
        e4 = sb("e4", [P, ES, C, NB], F32R)
        prod = sb("prod", [P, 4, C, NB])
        zT = sb("zT", [P, 2, NZ, NB])
        h1 = sb("h1", [P, H1 // P, NB])
        w1s = sb("w1s", [P, NZ, H1])
        w2s = sb("w2s", [P, H1 // P, H2])
        w3s = sb("w3s", [P, H2 // P])
        b1s = sb("b1s", [P, H1 // P])
        b2s = sb("b2s", [P, H2 // P])
        stage = sb("stage", [P, WS - 1, WP * P])
        sel = sb("sel", [P, SELW])
        ident = sb("ident", [P, P])
        dense_g = sb("dense_g", [P, TPG, DENSE])
        idx_a = sb("idx_a", [P, IDX_A * TPG], I32)
        idx_b = sb("idx_b", [P, (F - IDX_A) * TPG], I32)
        table = sb("table", [P, HOT, HK, D])
        row_of = sb("row_of", [P, HK])
        room = stage[0:HP, :, :].rearrange("p s n -> p (s n)").rearrange("p (s f n) -> p s f n", f=HOT, n=NB)
        hot_idx = room[:, 0].bitcast(I32)
        one_hot = room[:, 1:1 + OS]
        stages = [stage[:, r, :] for r in range(WS - 1)] + [h1[:, :, :].rearrange("p m n -> p (m n)")]
        h2 = zT[:, :, NZ - H2 // P:NZ, :]
        y_sb = h1[0:1, 0, :]

        scratch = nc.dram_tensor("scratch", (ES, C, 2, D, NB), F32, kind="Internal").ap()

        u_ps = ctx.enter_context(nc.psum_tensor("u_ps", [P, 2, C, NB], F32))
        z_ps = ctx.enter_context(nc.psum_tensor("z_ps", [P, 2, 2 * NB], F32))[:, :, 0:NB]
        t_ps = ctx.enter_context(nc.psum_tensor("t_ps", [P, 2 * NB], F32))[:, 0:NB]
        m_ps = ctx.enter_context(nc.psum_tensor("m_ps", [P, 2 * NB], F32))[:, 0:NB]

        end_ps = [m_ps[:, :], t_ps[:, :], z_ps[:, 0, :], u_ps[:, 1, 0, :],
                  u_ps[:, 0, 0, :], u_ps[:, 0, 2, :], u_ps[:, 1, 2, :]]

        s_const = sem("s_const")
        s_mlpw = sem("s_mlpw")
        s_idxa = sem("s_idxa")
        s_idxb = sem("s_idxb")
        s_dense = sem("s_dense")
        s_rows = [sem(f"s_rows{r}") for r in range(R)]
        s_tp = sem("s_tp")
        s_eh = sem("s_eh")
        s_et = sem("s_et")
        s_el = sem("s_el")
        s_scr = sem("s_scr")
        s_e4 = [sem(f"s_e4{r}") for r in range(ES)]
        s_stage = [sem(f"s_stage{r}") for r in range(WS)]
        s_wh = sem("s_wh")
        s_wl = sem("s_wl")
        s_held = sem("s_held")
        s_pad = sem("s_pad")
        s_u = sem("s_u")
        s_mul = sem("s_mul")
        s_red = sem("s_red")
        s_z = sem("s_z")
        s_zc = sem("s_zc")
        s_m = sem("s_m")
        s_mc = sem("s_mc")
        s_table = sem("s_table")
        s_hidx = sem("s_hidx")
        s_hot = sem("s_hot")
        s_look = sem("s_look")
        s_y = sem("s_y")

        ROWS = 16 * TPG
        E4 = 16 * 2
        E4_GROUP = E4 * NG // ES

        def rows_at(t, g, first):
            per_group = ROWS * sum(gathered(x, False) for x in range(g % R, NG, R))
            here = ROWS * sum(gathered(x, first) for x in range(g % R, g + 1, R))
            more_in_first = ROWS * HOT if g % R == HG % R and not first else 0
            return at(t, per_group, here + more_in_first)

        def e4_count(g):
            return E4 * (g // ES + 1)

        def e_slot(par, g):
            return NG + g if par and g < XE else g

        def hold(eng):
            eng.sem_inc(s_held, 1)

        block = ctx.enter_context(nc.Block())

        @block.gpsimd
        def _(pool):
            def group(t, first):
                for g in range(NG):
                    if g == 0:
                        pool.wait_ge(s_idxa, at(t, 16, 16))
                        hold(pool)
                    if C * g == IDX_A:
                        pool.wait_ge(s_idxb, at(t, 16, 16))
                        hold(pool)
                    if not first or g >= R:
                        pool.wait_ge(s_tp, at(t, NG, g - R + 1))
                        hold(pool)
                    for q in range(gathered(g, first)):
                        f = C * g + q
                        idx, col = (idx_a, f * TPG) if f < IDX_A else (idx_b, (f - IDX_A) * TPG)
                        for n in range(TPG):
                            pool.indirect_dma_start(
                                e_rows[:, g % R, n, D * q:D * q + D], None, tables[f],
                                bass.IndirectOffsetOnAxis(ap=idx[:, col + n:col + n + 1], axis=0),
                            ).then_inc(s_rows[g % R], 16)

            group(0, True)
            with pool.Fori(1, NT) as t:
                group(t, False)

        @block.sync
        def _(sp):
            def load_piece(k):
                if k >= NP:
                    return
                if k >= WS:
                    sp.wait_ge(s_wl, k - WS + 1)
                for r in range(4):
                    sp.dma_start(stages[k % WS][D * r:D * r + D, :],
                                 w[:, k * WP * P:(k + 1) * WP * P]).then_inc(s_stage[k % WS], 16)

            def stack_chunk(t, g, first):
                nj = fields_in(g)
                here = scratch[g % ES, 0:nj]
                if not first or g >= ES:
                    sp.wait_ge(s_e4[g % ES], at(t, E4_GROUP, e4_count(g) - E4))
                    hold(sp)
                sp.wait_ge(s_eh, at(t, NG, g + 1))
                hold(sp)
                sp.dma_start(here[:, 0], parts[0:D * nj, g % PS, 0, :].bitcast(F32)).then_inc(s_scr, 16)
                sp.wait_ge(s_el, at(t, NG, g + 1))
                hold(sp)
                sp.dma_start(here[:, 1], parts[0:D * nj, g % PS, 1, :].bitcast(F32)).then_inc(s_scr, 16)
                if not first or g >= ES:
                    sp.wait_ge(s_u, at(t, NS, FIRST_STEP[g - ES + 1] if g >= ES else FIRST_STEP[NG - ES + g + 1] - NS))
                    hold(sp)
                sp.wait_ge(s_scr, at(t, 32 * NG, 32 * (g + 1)))
                hold(sp)
                for r in range(2):
                    sp.dma_start(e4[2 * D * r:2 * D * (r + 1), g % ES, 0:nj, :].bitcast(F32),
                                 here.rearrange("j h a n -> (h a) j n")).then_inc(s_e4[g % ES], 16)

            def rows_of(array, t):
                return array[t:t + 1] if isinstance(t, int) else array[bass.ds(t, 1)]

            def load_indices(t, half):
                if half == 0:
                    sp.dma_start(idx_a[:, :], rows_of(ids, t)[:, :, 0:IDX_A * TPG].rearrange("t p n -> p (t n)")).then_inc(s_idxa, 16)
                else:
                    sp.dma_start(idx_b[:, :], rows_of(ids, t)[:, :, IDX_A * TPG:].rearrange("t p n -> p (t n)")).then_inc(s_idxb, 16)

            def load_hot_indices(t):
                sp.dma_start(hot_idx, rows_of(hot_ids, t).rearrange("t f n -> t (f n)").broadcast_to([HP, HOT * NB])
                             .rearrange("p (f n) -> p f n", f=HOT)).then_inc(s_hidx, 16)

            def group(t, first, last):
                if not first:
                    sp.wait_ge(s_z, at(t, 1, 0))
                    hold(sp)
                sp.dma_start(dense_g[:, :, :], rows_of(dense, t).rearrange("t p n d -> p (t n) d")).then_inc(s_dense, 16)
                for g in range(0 if first else AHEAD, NG):
                    stack_chunk(t, g, first)
                    if first and g < 2:
                        load_piece(g + WS)
                    elif first:
                        for n in range(START[g], START[g + 1]):
                            for k in pieces_at(n):
                                load_piece(k + WS)
                    if C * (g + 1) == IDX_A and not last:
                        load_indices(t + 1, 0)
                    if g == (BEFORE if first else NG - 1) and not last:
                        for x in range(IDX_A // C, NG):
                            sp.wait_ge(s_rows[x % R], rows_at(t, x, first))
                            hold(sp)
                        load_indices(t + 1, 1)
                    if g == HG + 1 and not first and not last:
                        sp.wait_ge(s_hot, at(t, HK, 0))
                        hold(sp)
                        load_hot_indices(t + 1)
                if first:
                    sp.wait_ge(s_wl, NP)
                    load_hot_indices(t + 1)
                if not last:
                    for g in range(AHEAD):
                        stack_chunk(t + 1, g, False)

            sp.dma_start(idx_a[:, :], ids[0, :, 0:IDX_A * TPG]).then_inc(s_idxa, 16)
            sp.dma_start(ident[:, :], ident_in).then_inc(s_const, 16)
            load_piece(0)
            sp.dma_start(sel[:, :], sel_in).then_inc(s_const, 16)
            load_piece(1)
            load_indices(0, 1)
            for k in range(2, WS):
                load_piece(k)
            sp.dma_start(row_of[:, :], hot_rows).then_inc(s_table, 16)
            for q in range(HOT):
                sp.dma_start(table[0:HP, q], tables[C * HG + C - HOT + q].rearrange("(p k) c -> p k c", k=HK)).then_inc(s_table, 16)
            group(0, True, False)
            with sp.Fori(1, NT - 1) as t:
                group(t, False, False)
            group(NT - 1, False, True)

        @block.tensor
        def _(pe):
            def transpose_chunk(t, g, first):
                pe.wait_ge(s_rows[g % R], rows_at(t, g, first))
                if not first or g >= 1:
                    pe.wait_ge(s_et, at(t, NG, g))
                n = D * gathered(g, first)
                for b in range(TPG):
                    last = nc.tensor.transpose(t_ps[0:n, b * P:b * P + P], e_rows[:, g % R, b, 0:n], ident[:, :])
                last.then_inc(s_tp, 1)

            def look_up_slice(t, k):
                if k == 0:
                    pe.wait_ge(s_table, 16 * (HOT + 1))
                    pe.wait_ge(s_et, at(t, NG, HG))
                pe.wait_ge(s_hot, at(t, HK, k + 1 - HK))
                for q in range(HOT):
                    row = D * (C - HOT + q)
                    last = nc.tensor.matmul(t_ps[row:row + D, :], table[0:HP, q, k, :], one_hot[:, k % OS, q, :],
                                            start=k == 0, stop=k == HK - 1, skip_group_check=True)
                last.then_inc(s_look, 1)

            def interact(t, n, first):
                g = UNITS[STEPS[n][0]][0]
                if n in FIRST_STEP:
                    pe.wait_ge(s_e4[g % ES], at(t, E4_GROUP, e4_count(g)))
                if first and (n == 0 or STEPS[n][-1] // WP > STEPS[n - 1][-1] // WP):
                    pe.wait_ge(s_wl, STEPS[n][-1] // WP + 1)
                if n >= 2:
                    pe.wait_ge(s_mul, at(t, NS, n - 1))
                for i, u in enumerate(STEPS[n]):
                    last = nc.tensor.matmul(u_ps[:, n % 2, i, :], w4[:, u, :], e4[:, g % ES, UNITS[u][2] - C * g, :],
                                            start=True, stop=True)
                last.then_inc(s_u, 1)

            def reduce(t, batch, first):
                pe.wait_ge(s_mul, at(t, NS, batch[-1] + 1))
                for n in batch:
                    for i, u in enumerate(STEPS[n]):
                        tile, quad, row = PLACES[u]
                        opens = (tile, quad) not in [x[:2] for x in PLACES[:u]]
                        closes = (tile, quad) not in [x[:2] for x in PLACES[u + 1:]]
                        if tile >= 2 and tile not in [x[0] for x in PLACES[:u]]:
                            pe.wait_ge(s_zc, at(t, NZ, tile - 1))
                        last = nc.tensor.matmul(z_ps[D * quad:D * quad + D, tile % 2, :],
                                                sel[:, D - 1 - row:2 * D - 1 - row], prod[:, n % 4, i, :],
                                                start=opens, stop=closes, skip_group_check=True)
                    last.then_inc(s_red, 1)

            def add_dense(t):
                pe.wait_ge(s_dense, at(t, 16, 16))
                for b in range(TPG):
                    last = nc.tensor.matmul(z_ps[0:DENSE, (NZ - 1) % 2, b * P:b * P + P], dense_g[:, b, :],
                                            ident[:, :], start=False, stop=False, skip_group_check=True)
                last.then_inc(s_z, 1)

            def mlp_piece(t, par, layer, m, k):
                if (layer, m, k) == (1, 0, 0):
                    pe.wait_ge(s_mlpw, 16 * 5)
                    pe.wait_ge(s_zc, at(t, NZ, NZ))
                elif k == 0:
                    pe.wait_ge(s_mc, at(t, NI, ITEM[layer, m]))
                stop = k == LAYER_INPUTS[layer] - 1
                if layer == 1:
                    last = nc.tensor.matmul(m_ps[:, :], w1s[:, k, m * P:m * P + P], zT[:, par, k, :], start=k == 0, stop=stop)
                elif layer == 2:
                    last = nc.tensor.matmul(m_ps[:, :], w2s[:, k, m * P:m * P + P], h1[:, k, :], start=k == 0, stop=stop)
                else:
                    last = nc.tensor.matmul(m_ps[0:1, :], w3s[:, k:k + 1], h2[:, par, k, :], start=k == 0, stop=stop)
                if stop:
                    last.then_inc(s_m, 1)

            def early_piece(t, par, m, k):
                if (m, k) == (0, 0):
                    pe.wait_ge(s_mc, at(t, NI, 0))
                if (m, k) == (1, 0):
                    pe.wait_ge(s_et, at(t, NG, NG))
                pe.wait_ge(s_zc, at(t, NZ, NZ - 1 if m == 2 else k + 1))
                if (m, k) == (3, 0):
                    pe.wait_ge(s_mul, at(t, NS, NS - 1))
                nc.tensor.matmul(end_ps[m], w1s[:, k, m * P:m * P + P], zT[:, par, k, :], start=k == 0, stop=False)

            def finish(t, par):
                for m in range(H1 // P):
                    if m == 0:
                        pe.wait_ge(s_zc, at(t, NZ, NZ))
                    nc.tensor.matmul(end_ps[m], w1s[:, NZ - 1, m * P:m * P + P], zT[:, par, NZ - 1, :],
                                     start=False, stop=True).then_inc(s_m, 1)
                for k in range(H1 // P):
                    pe.wait_ge(s_mc, at(t, NI, k + 1))
                    for m in range(H2 // P):
                        last = nc.tensor.matmul(end_ps[ITEM[2, m]], w2s[:, k, m * P:m * P + P], h1[:, k, :],
                                                start=k == 0, stop=k == H1 // P - 1)
                        if k == H1 // P - 1:
                            last.then_inc(s_m, 1)
                for k in range(H2 // P):
                    pe.wait_ge(s_mc, at(t, NI, ITEM[2, k] + 1))
                    last = nc.tensor.matmul(end_ps[ITEM[3, 0]][0:1, :], w3s[:, k:k + 1], h2[:, par, k, :],
                                            start=k == 0, stop=k == H2 // P - 1)
                last.then_inc(s_m, 1)

            def group(t, par, first, last):
                chunks = bring(first, last)
                if first:
                    transpose_chunk(t, 0, first)
                    transpose_chunk(t, 1, first)
                for n in range(0, NS + BS, BS):
                    for x in range(n, min(n + BS, NS)):
                        for g in chunks.get(x, ()):
                            transpose_chunk(t, g, first)
                        for k in range(0 if first else HK):
                            if look_up(last)[k] == x:
                                look_up_slice(t, k)
                        if x in NEXT and not last:
                            transpose_chunk(t + 1, NEXT[x], False)
                        interact(t, x, first)
                        if not first:
                            pieces = mlp_pieces(n // BS, last)
                            for piece in pieces[len(pieces) * (x - n) // BS:len(pieces) * (x - n + 1) // BS]:
                                mlp_piece(t - 1, 1 - par, *piece)
                    if n >= NS:
                        add_dense(t)
                    if n >= BS:
                        reduce(t, range(n - BS, min(n, NS)), first)
                    if last:
                        for m, k in EARLY.get(n // BS, ()):
                            early_piece(t, par, m, k)

            pe.wait_ge(s_const, 32)
            group(0, 0, True, False)
            with pe.Fori(0, (NT - 2) // 2) as pair:
                group(2 * pair + 1, 1, False, False)
                group(2 * pair + 2, 0, False, False)
            group(NT - 1, 1, False, True)
            finish(NT - 1, (NT - 1) % 2)

        @block.scalar
        def _(act):
            def take_chunk(t, par, g, first):
                n = D * fields_in(g)
                if not first or g >= PS:
                    act.wait_ge(s_scr, at(t, 32 * NG, 32 * (g - PS + 1)))
                act.wait_ge(s_tp, at(t, NG, g + 1))
                nc.scalar.copy(parts[0:n, g % PS, 0, :], t_ps[0:n, :]).then_inc(s_eh, 1)
                if g >= XE and not first:
                    act.wait_ge(s_mul, at(t, NS, last_step_with(g) + 1 - NS))
                elif g < XE and not (isinstance(t, int) and t < 2):
                    act.wait_ge(s_mul, at(t, NS, last_step_with(g) + 1 - 2 * NS))
                nc.scalar.copy(eT[0:n, e_slot(par, g), :], t_ps[0:n, :]).then_inc(s_et, 1)

            def weights_high(k):
                act.wait_ge(s_stage[k % WS], 64 * (k // WS + 1))
                nc.scalar.copy(w4[:, k * WP:(k + 1) * WP, :].rearrange("p u n -> p (u n)"),
                               stages[k % WS]).then_inc(s_wh, 1)

            def take_z(t, par, tile):
                act.wait_ge(s_red, at(t, NS, last_step_of_tile(tile) + 1))
                nc.scalar.copy(zT[:, par, tile, :], z_ps[:, tile % 2, :]).then_inc(s_zc, 1)

            def take_mlp(t, par, layer, m, src, dst):
                act.wait_ge(s_m, at(t, NI, ITEM[layer, m] + 1))
                if layer == 1:
                    nc.scalar.activation(h1[:, m, :], src, ACT.Relu, bias=b1s[:, m:m + 1]).then_inc(s_mc, 1)
                elif layer == 2:
                    nc.scalar.activation(h2[:, par, m, :], src, ACT.Relu, bias=b2s[:, m:m + 1]).then_inc(s_mc, 1)
                else:
                    nc.scalar.copy(y_sb, src[0:1, :]).then_inc(s_mc, 1)
                    act.wait_ge(s_mc, at(t, NI, NI))
                    act.sem_inc(s_held, 1)
                    act.dma_start(dst, y_sb).then_inc(s_y, 16)

            def group(t, par, first, last):
                chunks = bring(first, last)
                if first:
                    for g in (0, 1):
                        take_chunk(t, par, g, first)
                        weights_high(g)
                for n in range(0, NS + BS, BS):
                    for x in range(n, n + BS):
                        for g in chunks.get(x, ()):
                            take_chunk(t, par, g, first)
                        if first:
                            for k in pieces_at(x):
                                weights_high(k)
                        if x in NEXT and not last:
                            take_chunk(t + 1, 1 - par, NEXT[x], False)
                    if not first:
                        for layer, m, k in mlp_pieces(n // BS, last):
                            if k == LAYER_INPUTS[layer] - 1:
                                take_mlp(t - 1, 1 - par, layer, m, m_ps[:, :], y[t - 1:t, :] if last else y[bass.ds(t - 1, 1), :])
                    for tile in range(NZ - 1):
                        if last_step_of_tile(tile) // BS + 1 == n // BS:
                            take_z(t, par, tile)
                take_z(t, par, NZ - 1)
                if not first:
                    act.wait_ge(s_y, at(t, 16, 0))

            for dst, src in ((w1s[:, :, :], w1), (w2s[:, :, :], w2), (w3s[:, :], w3), (b1s[:, :], b1), (b2s[:, :], b2)):
                act.dma_start(dst, src).then_inc(s_mlpw, 16)
            group(0, 0, True, False)
            act.wait_ge(s_mlpw, 16 * 5)
            with act.Fori(0, (NT - 2) // 2) as pair:
                group(2 * pair + 1, 1, False, False)
                group(2 * pair + 2, 0, False, False)
            group(NT - 1, 1, False, True)
            for layer, m in ITEM:
                take_mlp(NT - 1, (NT - 1) % 2, layer, m, end_ps[ITEM[layer, m]], y[NT - 1:NT, :])
            act.wait_ge(s_y, 16 * NT)

        @block.vector
        def _(dve):
            def split_chunk(t, par, g):
                n = D * fields_in(g)
                dve.wait_ge(s_et, at(t, NG, g + 1))
                nc.vector.tensor_tensor(parts[0:n, g % PS, 1, :], eT[0:n, e_slot(par, g), :], parts[0:n, g % PS, 0, :].bitcast(F32),
                                        ALU.subtract).then_inc(s_el, 1)

            def weights_low(k):
                dve.wait_ge(s_wh, k + 1)
                piece = w4[P // 2:P, k * WP:(k + 1) * WP, :].rearrange("p u n -> p (u n)")
                nc.vector.tensor_tensor(piece, stages[k % WS][P // 2:P, :], piece.bitcast(F32),
                                        ALU.subtract).then_inc(s_wl, 1)

            def one_hot_slice(t, k):
                if k == 0:
                    dve.wait_ge(s_table, 16 * (HOT + 1))
                    dve.wait_ge(s_hidx, at(t, 16, 0))
                if k >= OS:
                    dve.wait_ge(s_look, at(t, HK, k - OS + 1 - HK))
                nc.vector.tensor_scalar(one_hot[:, k % OS], hot_idx, row_of[0:HP, k:k + 1], None,
                                        ALU.is_equal).then_inc(s_hot, 1)

            def multiply(t, par, n, first):
                dve.wait_ge(s_u, at(t, NS, n + 1))
                if n >= 4:
                    dve.wait_ge(s_red, at(t, NS, n - 3))
                elif n == 0 and not first:
                    dve.wait_ge(s_red, at(t, NS, 0))
                k = len(STEPS[n])
                gi = e_slot(par, UNITS[STEPS[n][0]][1])
                e = eT[:, gi:gi + 1, :].broadcast_to([P, k, NB])
                nc.vector.tensor_tensor(prod[:, n % 4, 0:k, :], u_ps[:, n % 2, 0:k, :], e,
                                        ALU.mult).then_inc(s_mul, 1)

            def group(t, par, first, last):
                chunks = bring(first, last)
                if first:
                    for g in (0, 1):
                        split_chunk(t, par, g)
                        weights_low(g)
                for n in range(NS):
                    for g in chunks.get(n - SPLIT_LAG, ()):
                        split_chunk(t, par, g)
                    if first:
                        for k in pieces_at(n):
                            weights_low(k)
                    for k in range(0 if first else HK):
                        if look_up(last)[k] - HOT_LEAD == n:
                            one_hot_slice(t, k)
                    if n - NEXT_LAG in NEXT and not last:
                        split_chunk(t + 1, 1 - par, NEXT[n - NEXT_LAG])
                    multiply(t, par, n, first)

            nc.vector.memset(eT[D * fields_in(NG - 1):P, NG - 1, :], 0.0).then_inc(s_pad, 1)
            dve.wait_ge(s_pad, 1)
            group(0, 0, True, False)
            with dve.Fori(0, (NT - 2) // 2) as pair:
                group(2 * pair + 1, 1, False, False)
                group(2 * pair + 2, 0, False, False)
            group(NT - 1, 1, False, True)


def kernel(**inputs):
    import numpy as _np
    import concourse.bacc as _bacc
    from concourse import mybir as _mybir
    from concourse.bass_utils import run_bass_kernel_spmd as _run

    nc = _bacc.Bacc("TRN2", target_bir_lowering=False, num_devices=1)
    arrays = {}

    def give(name, a):
        a = _np.ascontiguousarray(a)
        arrays[f"in_{name}_dram"] = a
        return nc.dram_tensor(f"in_{name}_dram", a.shape, _mybir.dt.from_np(a.dtype), kind="ExternalInput").ap()

    tables = [give(f"tbl_{f}", inputs[f"tbl_{f}"]) for f in range(F)]

    ids = _np.asarray(inputs["ids"])
    ids_in = give("ids", ids.reshape(NT, TPG, P, F).transpose(0, 2, 3, 1).reshape(NT, P, F * TPG))
    hot_fields = slice(C * HG + C - HOT, C * HG + C)
    hot_ids = give("hot_ids", ids[:, hot_fields].reshape(NT, NB, HOT).transpose(0, 2, 1))
    hot_rows = give("hot_rows", (_np.arange(P)[:, None] * HK + _np.arange(HK)).astype(_np.float32))
    dense = _np.asarray(inputs["dense_ctx"]).reshape(NT, TPG, P, DENSE).transpose(0, 2, 1, 3)
    dense_in = give("dense", dense)

    w = _np.asarray(inputs["L0_rec_w"])
    w1 = _np.asarray(inputs["W_top1"])
    w_units = _np.zeros((D, NU, C, D), w.dtype)
    w1_rows = _np.zeros((NZ * P, H1), w1.dtype)
    for u, (g, gi, j) in enumerate(UNITS):
        tile, quad, row = PLACES[u]
        for q in range(min(C, j - C * gi)):
            i = C * gi + q
            pair = i * F - i * (i + 1) // 2 + j - i - 1
            w_units[:, u, q, :] = w[:, pair, :]
            w1_rows[tile * P + D * quad + row + q] = w1[pair]
    w1_rows[(NZ - 1) * P:(NZ - 1) * P + DENSE] = w1[PAIRS:]
    w_in = give("w", w_units.reshape(D, NU * P))
    w1_in = give("w1", w1_rows.reshape(NZ, P, H1).transpose(1, 0, 2))
    w2_in = give("w2", _np.asarray(inputs["W_top2"]).reshape(H1 // P, P, H2).transpose(1, 0, 2))
    w3_in = give("w3", _np.asarray(inputs["W_top3"]).reshape(H2 // P, P).T)
    b1_in = give("b1", _np.asarray(inputs["b_top1"]).reshape(H1 // P, P).T)
    b2_in = give("b2", _np.asarray(inputs["b_top2"]).reshape(H2 // P, P).T)

    sel = _np.zeros((P, SELW), _np.float32)
    for p in range(P):
        sel[p, D - 1 + p // D] = 1.0
    sel_in = give("sel", sel)
    ident_in = give("ident", _np.eye(P, dtype=_np.float32))

    y = nc.dram_tensor("out_y_dram", (NT, NB), _mybir.dt.float32, kind="ExternalOutput").ap()
    tower(nc, tables, ids_in, hot_ids, hot_rows, dense_in, w_in, w1_in, b1_in, w2_in, b2_in, w3_in, sel_in, ident_in, y)
    r = _run(nc, [arrays], core_ids=[0])
    return r.results[0]["out_y_dram"].reshape(B, 1)
```
